# Optimizing a Trainium2 kernel written in Bass

```python
import numpy as np
import jax
import jax.numpy as jnp

def _softmax(x, axis=-1):
    return jax.nn.softmax(x, axis=axis)

def _gelu(x):
    return jax.nn.gelu(x, approximate=True)

def _silu(x):
    return jax.nn.silu(x)

def _sigmoid(x):
    return jax.nn.sigmoid(x)

def _layernorm(x, axis=-1, eps=1e-05):
    m = jnp.mean(x, axis=axis, keepdims=True)
    v = jnp.var(x, axis=axis, keepdims=True)
    return (x - m) / jnp.sqrt(v + eps)

def _scatter_add(tgt, idx, src, axis=0):
    return tgt.at[idx].add(src)

def _segment_sum(src, seg, n):
    return jax.ops.segment_sum(src, seg, n)
kernel_name = 'mk_gnn_preln_d4_gnn_r16_862137'

def setup_inputs(seed: int=0):
    np.random.seed(seed)
    _w = jnp.asarray

    def _rec_inputs():
        import jax
        import jax.numpy as jnp
        _gk = jax.random.key(seed)
        x = -0.0003713 + 1 * jax.random.normal(jax.random.fold_in(_gk, 1), (6250, 128), jnp.float32)
        _s = jax.random.randint(jax.random.fold_in(_gk, 2), (100000,), 0, 6250, jnp.int32)
        _d = jax.random.randint(jax.random.fold_in(_gk, 3), (100000,), 0, 6250, jnp.int32)
        _loop = jnp.arange(6250, dtype=jnp.int32)
        src = jnp.concatenate([_s, _d, _loop])
        dst = jnp.concatenate([_d, _s, _loop])
        _o = jnp.argsort(dst, stable=True)
        src = src[_o]
        dst = dst[_o]
        edge_weight = jax.random.uniform(jax.random.fold_in(_gk, 13), (206250,), jnp.float32, 0.0, 1)
        return (x, src, dst, edge_weight)
    x, src, dst, edge_weight = _rec_inputs()

    def _L0_gnn_setup():
        import jax, jax.numpy as jnp
        import numpy as np
        N_NODES = 6250
        N_EDGES = 100000
        D_FEAT = 128
        UNITS = 128
        key = jax.random.key(seed)
        k = jax.random.split(key, 7)
        x = jax.random.normal(k[0], (N_NODES, D_FEAT), dtype=jnp.float32)
        edge_row = jax.random.randint(k[1], (N_EDGES,), 0, N_NODES, dtype=jnp.int32)
        edge_col = jax.random.randint(k[2], (N_EDGES,), 0, N_NODES, dtype=jnp.int32)
        edge_vals = jax.random.uniform(k[3], (N_EDGES,), dtype=jnp.float32)
        W = jax.random.normal(k[4], (D_FEAT, UNITS), dtype=jnp.float32) * 0.05
        W_gate = jax.random.normal(k[5], (D_FEAT, 1), dtype=jnp.float32) * 0.05
        b_gate = jax.random.normal(k[6], (1,), dtype=jnp.float32) * 0.05
        return {'x': x, 'edge_row': edge_row, 'edge_col': edge_col, 'edge_vals': edge_vals, 'W': W, 'W_gate': W_gate, 'b_gate': b_gate}
    _L0_gnn_all = _L0_gnn_setup()
    _L0_gnn_in = {k: v for k, v in _L0_gnn_all.items() if k in ('W', 'W_gate', 'b_gate')}
    del _L0_gnn_all

    def _L1_gnn_setup():
        import jax, jax.numpy as jnp
        import numpy as np
        NUM_NODES = 3125
        IN_CH = 128
        OUT_CH = 128
        NUM_EDGES = 37500
        key = jax.random.key(seed)
        k_x, k_e, k_w, k_b = jax.random.split(key, 4)
        x = jax.random.normal(k_x, (NUM_NODES, IN_CH), dtype=jnp.float32)
        edge_index = jax.random.randint(k_e, (2, NUM_EDGES), 0, NUM_NODES, dtype=jnp.int32)
        bound = 1.0 / np.sqrt(IN_CH)
        W = jax.random.uniform(k_w, (OUT_CH, IN_CH), minval=-bound, maxval=bound, dtype=jnp.float32)
        b = jax.random.uniform(k_b, (OUT_CH,), minval=-bound, maxval=bound, dtype=jnp.float32)
        return {'x': x, 'edge_index': edge_index, 'W': W, 'b': b}
    _L1_gnn_all = _L1_gnn_setup()
    _L1_gnn_in = {k: v for k, v in _L1_gnn_all.items() if k in ('W', 'b')}
    del _L1_gnn_all

    def _L2_gnn_setup():
        import jax, jax.numpy as jnp
        import numpy as np
        N_ATOMS = 625
        N_EDGES = 40000
        IN_F = 128
        OUT_F = 128
        key = jax.random.key(seed)
        k1, k2, k3, k4, k5, k6 = jax.random.split(key, 6)
        atom_features = jax.random.normal(k1, (N_ATOMS, IN_F), dtype=jnp.float32)
        edge_indices = jax.random.randint(k2, (2, N_EDGES), 0, N_ATOMS, dtype=jnp.int64)
        bm_lim = 1.0 / np.sqrt(IN_F * 2)
        bu_lim = 1.0 / np.sqrt(IN_F + OUT_F)
        W_msg = jax.random.uniform(k3, (IN_F * 2, OUT_F), jnp.float32, -bm_lim, bm_lim)
        b_msg = jax.random.uniform(k4, (OUT_F,), jnp.float32, -bm_lim, bm_lim)
        W_upd = jax.random.uniform(k5, (IN_F + OUT_F, OUT_F), jnp.float32, -bu_lim, bu_lim)
        b_upd = jax.random.uniform(k6, (OUT_F,), jnp.float32, -bu_lim, bu_lim)
        return {'atom_features': atom_features, 'edge_indices': edge_indices, 'W_msg': W_msg, 'b_msg': b_msg, 'W_upd': W_upd, 'b_upd': b_upd}
    _L2_gnn_all = _L2_gnn_setup()
    _L2_gnn_in = {k: v for k, v in _L2_gnn_all.items() if k in ('W_msg', 'b_msg', 'W_upd', 'b_upd')}
    del _L2_gnn_all

    def _L3_gnn_setup():
        import jax, jax.numpy as jnp
        import numpy as np
        N, M, E = (3125, 6250, 50000)
        F_IN, F_OUT = (128, 128)
        BN_EPS = 1e-05
        key = jax.random.key(seed)
        ks = jax.random.split(key, 7)
        x = jax.random.normal(ks[0], (N, F_IN), dtype=jnp.float32)
        row = jax.random.randint(ks[1], (E,), 0, N)
        col = jax.random.randint(ks[2], (E,), 0, M)
        hyperedge_index = jnp.stack([row, col]).astype(jnp.int32)
        hyperedge_weight = jax.random.uniform(ks[3], (M,), dtype=jnp.float32) + 0.5
        W = jax.random.normal(ks[4], (F_IN, F_OUT), dtype=jnp.float32) / np.sqrt(F_IN)
        b = jax.random.normal(ks[5], (F_OUT,), dtype=jnp.float32) * 0.02
        gamma = jnp.ones((F_OUT,), dtype=jnp.float32)
        beta = jnp.zeros((F_OUT,), dtype=jnp.float32)
        return {'x': x, 'hyperedge_index': hyperedge_index, 'hyperedge_weight': hyperedge_weight, 'W': W, 'b': b, 'gamma': gamma, 'beta': beta}
    _L3_gnn_all = _L3_gnn_setup()
    _L3_gnn_in = {k: v for k, v in _L3_gnn_all.items() if k in ('hyperedge_weight', 'W', 'b', 'gamma', 'beta')}
    del _L3_gnn_all
    return {'x': x, 'src': src, 'dst': dst, 'edge_weight': edge_weight, 'L0_gnn_W': _L0_gnn_in['W'], 'L0_gnn_W_gate': _L0_gnn_in['W_gate'], 'L0_gnn_b_gate': _L0_gnn_in['b_gate'], 'L1_gnn_W': _L1_gnn_in['W'], 'L1_gnn_b': _L1_gnn_in['b'], 'L2_gnn_W_msg': _L2_gnn_in['W_msg'], 'L2_gnn_b_msg': _L2_gnn_in['b_msg'], 'L2_gnn_W_upd': _L2_gnn_in['W_upd'], 'L2_gnn_b_upd': _L2_gnn_in['b_upd'], 'L3_gnn_hyperedge_weight': _L3_gnn_in['hyperedge_weight'], 'L3_gnn_W': _L3_gnn_in['W'], 'L3_gnn_b': _L3_gnn_in['b'], 'L3_gnn_gamma': _L3_gnn_in['gamma'], 'L3_gnn_beta': _L3_gnn_in['beta']}

def reference(x, src, dst, edge_weight, L0_gnn_W, L0_gnn_W_gate, L0_gnn_b_gate, L1_gnn_W, L1_gnn_b, L2_gnn_W_msg, L2_gnn_b_msg, L2_gnn_W_upd, L2_gnn_b_upd, L3_gnn_hyperedge_weight, L3_gnn_W, L3_gnn_b, L3_gnn_gamma, L3_gnn_beta):
    import jax
    import jax.numpy as jnp

    def _L0_gnn_ref(x, edge_row, edge_col, edge_vals, W, W_gate, b_gate):
        import jax, jax.numpy as jnp
        import numpy as np
        N_NODES = 6250
        N_EDGES = 100000
        D_FEAT = 128
        UNITS = 128
        pre_sup = x @ W
        g = jax.nn.sigmoid(x @ W_gate + b_gate)
        h = g * pre_sup
        msgs = edge_vals[:, None] * h[edge_col]
        out = jax.ops.segment_sum(msgs, edge_row, num_segments=N_NODES)
        return out

    def _L1_gnn_ref(x, edge_index, W, b):
        import jax, jax.numpy as jnp
        import numpy as np
        NUM_NODES = 3125
        IN_CH = 128
        OUT_CH = 128
        NUM_EDGES = 37500
        src, dst = (edge_index[0], edge_index[1])
        agg = jax.ops.segment_sum(x[src], dst, num_segments=x.shape[0])
        return jnp.einsum('nc,oc->no', agg, W) + b

    def _L2_gnn_ref(atom_features, edge_indices, W_msg, b_msg, W_upd, b_upd):
        import jax, jax.numpy as jnp
        import numpy as np
        N_ATOMS = 625
        N_EDGES = 40000
        IN_F = 128
        OUT_F = 128
        src, dst = (edge_indices[0], edge_indices[1])
        edge_in = jnp.concatenate([atom_features[src], atom_features[dst]], axis=-1)
        messages = edge_in @ W_msg + b_msg
        agg = jax.ops.segment_sum(messages, dst, num_segments=atom_features.shape[0])
        upd_in = jnp.concatenate([atom_features, agg], axis=-1)
        return upd_in @ W_upd + b_upd

    def _L3_gnn_ref(x, hyperedge_index, hyperedge_weight, W, b, gamma, beta):
        import jax, jax.numpy as jnp
        import numpy as np
        N, M, E = (3125, 6250, 50000)
        F_IN, F_OUT = (128, 128)
        BN_EPS = 1e-05
        row = hyperedge_index[0]
        col = hyperedge_index[1]
        num_nodes = x.shape[0]
        num_edges = hyperedge_weight.shape[0]
        h = x @ W
        D = jax.ops.segment_sum(hyperedge_weight[col], row, num_segments=num_nodes)
        D_inv = jnp.where(D > 0, 1.0 / D, 0.0)
        B = jax.ops.segment_sum(jnp.ones_like(col, dtype=h.dtype), col, num_segments=num_edges)
        B_inv = jnp.where(B > 0, 1.0 / B, 0.0)
        e_feat = B_inv[:, None] * jax.ops.segment_sum(h[row], col, num_segments=num_edges)
        out = D_inv[:, None] * jax.ops.segment_sum(e_feat[col], row, num_segments=num_nodes)
        out = out + b
        mean = out.mean(axis=0)
        var = out.var(axis=0)
        out = gamma * (out - mean) * jax.lax.rsqrt(var + BN_EPS) + beta
        return jax.nn.relu(out)
    edge_index = jnp.stack([src, dst])
    h = jnp.maximum(_layernorm(x, axis=-1), 0.0)
    x = x + _L0_gnn_ref(h, src, dst, edge_weight, L0_gnn_W, L0_gnn_W_gate, L0_gnn_b_gate)
    h = jnp.maximum(_layernorm(x, axis=-1), 0.0)
    x = x + _L1_gnn_ref(h, edge_index, L1_gnn_W, L1_gnn_b)
    h = jnp.maximum(_layernorm(x, axis=-1), 0.0)
    x = x + _L2_gnn_ref(h, edge_index, L2_gnn_W_msg, L2_gnn_b_msg, L2_gnn_W_upd, L2_gnn_b_upd)
    h = jnp.maximum(_layernorm(x, axis=-1), 0.0)
    x = x + _L3_gnn_ref(h, edge_index, L3_gnn_hyperedge_weight, L3_gnn_W, L3_gnn_b, L3_gnn_gamma, L3_gnn_beta)
    return x

_drawn_inputs = setup_inputs


def setup_inputs(seed=0):
    import zlib

    import numpy as np

    out = dict(_drawn_inputs(seed))
    spreads = {'L3_gnn_gamma': (1.0, 0.6), 'L3_gnn_beta': (0.0, 0.8)}
    factors = {'L1_gnn_b': 8.0, 'L2_gnn_b_upd': 8.0, 'L3_gnn_b': 8.0}
    for name, (base, spread) in spreads.items():
        noise = np.random.default_rng([zlib.crc32(name.encode()), seed]).standard_normal(out[name].shape)
        drawn = base * np.exp(spread * noise) if base else spread * noise
        out[name] = jnp.asarray(drawn.astype(out[name].dtype))
    for name, factor in factors.items():
        out[name] = (out[name] * factor).astype(out[name].dtype)
    return out
```

```python
from contextlib import ExitStack

import concourse.bass as bass
import numpy as np
from concourse import mybir
from concourse.bass import IndirectOffsetOnAxis

F32, I32, BF16, F16 = mybir.dt.float32, mybir.dt.int32, mybir.dt.bfloat16, mybir.dt.float16
ALU = mybir.AluOpType
ACT = mybir.ActivationFunctionType
AX = mybir.AxisListType

P = 128
NODES, EDGES = 6250, 206250
TILES = -(-NODES // P)
LAST = NODES - (TILES - 1) * P
WD = 2
WCOLS = WD * TILES
GROUPS = 25
WINDOWS = GROUPS * P
HOT = 8
TILE_HOTS = P // WD // HOT
HALF = HOT // 2
ALIGN = 16
SAMPLES = 101
RUN = ALIGN * SAMPLES
ROWS = P * SAMPLES
PADDED = ROWS * ALIGN + P
NO_NODE = 16384
FITS = P // ALIGN - 1
LOW = 2048.0
WIDE = P + 2
CHUNKS = -(-EDGES // P)
PARTS = 2 * P + 2
EPS = 1e-5
SLOTS = 4
SET = 7
FOURS = -(-TILES // 4)
ESIZE = {F32: 4, I32: 4, BF16: 2, F16: 2}


def row(t, j):
    if isinstance(j, int):
        return t[:, j]
    return t[:, bass.ds(j, 1)].rearrange("p a f -> p (a f)")


def slab(t, j):
    if isinstance(j, int):
        return t[j]
    return t[bass.ds(j, 1)].rearrange("a p n -> (a p) n")


def on(j, lag=0):
    return not isinstance(j, int) or 0 <= j - lag < TILES


def later(j, n):
    return not isinstance(j, int) or j >= n


def turned_at(h):
    return range(2 * h, min(2 * h + 2, FOURS))


def summed_at(h):
    return turned_at(h - 1) if h else range(0)


def tiles_loop(eng, body, lag):
    peel = SLOTS + 1
    for j in range(peel):
        body(j, 0, j)
    with eng.Fori(0, (TILES - peel) // SLOTS) as k:
        for u in range(SLOTS):
            body(k * SLOTS + (peel + u), k, peel + u)
    for j in range(TILES, TILES + lag):
        body(j, 0, j)


def tiles_before(ph, q):
    return (ph - 1) * len(range(q, TILES, SLOTS))


def pairs_loop(eng, body):
    for j in range(3):
        body(j, j % 2, j // 2)
    with eng.Fori(0, (TILES - 3) // 2) as k:
        body(k * 2 + 3, 1, k + 1)
        body(k * 2 + 4, 0, k + 2)


class Chain:

    def __init__(self, eng, sem, start=0):
        self.eng, self.sem, self.start, self.n = eng, sem, start, 0

    def __call__(self, ins):
        self.n += 1
        ins.then_inc(self.sem, 1)
        self.eng.wait_ge(self.sem, self.start + self.n)


def gnn_kernel(nc, x, src, dst, edge_weight, w0, wg0, bg0, w1, b1, wm, bm, wu, bu, hyper, w3, b3, gamma, beta, out):
    ctx = ExitStack()
    with ctx:
        sems = {}

        def s(name):
            if name not in sems:
                sems[name] = ctx.enter_context(nc.semaphore(name))
            return sems[name]

        place = [16512]

        def at(name, shape, dt, offset):
            size = int(np.prod(shape[1:])) * ESIZE[dt]
            return nc.alloc_sbuf_tensor_at(name, shape, dt, offset=offset), offset + -(-size // 32) * 32

        def keep(name, shape, dt):
            t, place[0] = at(name, shape, dt, place[0])
            return t

        src_pad = nc.dram_tensor("src_pad", (PADDED,), I32).ap()
        dst_pad = nc.dram_tensor("dst_pad", (PADDED,), I32).ap()
        w_pad = nc.dram_tensor("w_pad", (PADDED,), I32).ap()
        table = nc.dram_tensor("edge_table", (ROWS, 3 * P), I32).ap()
        a_dram = nc.dram_tensor("counts", (TILES, P, TILES * P), F16).ap()
        at_dram = nc.dram_tensor("counts_t", (TILES, P, TILES * P), F16).ap()

        X = keep("X", [P, TILES, P], F32)
        ident = keep("ident", [P, P], F32)
        ident16 = keep("ident16", [P, P], F16)
        w0g = keep("w0g", [P, P + 1], F32)
        w1t = keep("w1t", [P, P], F32)
        w3s = keep("w3s", [P, P], F32)
        w_h = keep("w_h", [P, 2, P], F32)
        w_s = keep("w_s", [P, P], F32)
        b1s = keep("b1s", [P, P], F32)
        bus = keep("bus", [P, P], F32)
        bmu = keep("bmu", [P, P], F32)
        cols = keep("cols", [P, 8], F32)
        stats = keep("stats", [P, TILES, 6], F32)
        mv = keep("mv", [P, TILES, 2], F32)
        rstd = keep("rstd", [P, TILES], F32)
        nmr = keep("nmr", [P, TILES], F32)
        extra = keep("extra", [P, TILES, 2], F32)
        indeg = keep("indeg", [P, TILES], F32)
        binv = keep("binv", [P, TILES], F32)
        hyp = keep("hyp", [P, TILES], F32)
        t49 = keep("t49", [P, 3, TILES], F32)
        small = keep("small", [P, SLOTS, 8], F32)
        flag = keep("flag", [P, 1], I32)
        fin = keep("fin", [P, 8], F32)
        base0 = place[0]

        meta, o = at("meta", [P, 5, WINDOWS], BF16, base0)
        H0, o = at("H0", [P, TILES, P], F32, o)
        iota_r, o = at("iota_r", [P, P, HOT], BF16, o)
        iota_c, o = at("iota_c", [P, WCOLS, HOT], BF16, o)
        base1 = o
        hot_r, o = at("hot_r", [P, 2, P, HOT], BF16, o)
        hot_c, o = at("hot_c", [P, 2, 4, WCOLS, HOT], BF16, o)
        wt, o = at("wt", [P, 2, 4, P], F32, o)
        stage_w, o = at("stage_w", [P, 2, TILES, P], F32, o)
        stage_a, o = at("stage_a", [P, 2, TILES, P], F16, o)
        assert o <= nc.sbuf_usable_end, o
        dst_run, o = at("dst_run", [P, RUN + 1], I32, base1)
        viol, o = at("viol", [P, RUN], BF16, o)
        smp, o = at("smp", [P, 2, SAMPLES], I32, o)
        smpf, o = at("smpf", [P, 2, SAMPLES], BF16, o)
        hot_b, o = at("hot_b", [P, SAMPLES, P], BF16, o)
        hot_g, o = at("hot_g", [P, SAMPLES, GROUPS], BF16, o)
        io_b, o = at("io_b", [P, P], BF16, o)
        before, o = at("before", [P, P], F32, o)
        ones, o = at("ones", [P, P], F32, o)
        hist, o = at("hist", [P, GROUPS], F32, o)
        tot, o = at("tot", [P, 3, GROUPS], F32, o)
        bad, o = at("bad", [P, 4], F32, o)
        first, o = at("first", [P, GROUPS], I32, o)
        basei, o = at("basei", [P, GROUPS], I32, o)
        basef, o = at("basef", [P, GROUPS], F32, o)
        diff, o = at("diff", [P, P], I32, o)
        rec, o = at("rec", [P, GROUPS, 3 * P], I32, o)
        ri, o = at("ri", [P, 5, 2, P], I32, o)
        pre, o = at("pre", [P, 5, 3, P], F32, o)
        wres, o = at("wres", [P, 5, 2, P], F32, o)
        pad_rows, o = at("pad_rows", [1, 2, PADDED - EDGES], I32, o)
        wraw, o = at("wraw", [P, 7, P], F32, o)
        hrows, o = at("hrows", [P, P], F32, o)
        hs0, o = at("hs0", [P, SLOTS, P], F32, o)
        hts0, o = at("hts0", [P, SLOTS, P], F32, o)
        assert o <= nc.sbuf_usable_end, o
        h_dram = nc.dram_tensor("gathered_rows", (TILES * P, WIDE), F32).ap()
        Ha, o = at("Ha", [P, TILES, PARTS], F16, base0)
        Hb, o = at("Hb", [P, TILES, PARTS], F16, o)
        a_tiles, o = at("a_tiles", [P, SLOTS, TILES, P], F16, o)
        low, o = at("low", [P, SLOTS, P], F32, o)
        agg, o = at("agg", [P, SLOTS, P], F32, o)
        aggt, o = at("aggt", [P, SLOTS, 2, P], F32, o)
        hrow, o = at("hrow", [P, SLOTS, P], F32, o)
        upd, o = at("upd", [P, SLOTS, 2, P], F32, o)
        t_stage, _ = at("t_stage", [P, 2, TILES, 2, P], F16, o)
        hbig, o2 = at("hbig", [P, 2, SET, P], F32, o)
        dbig, _ = at("dbig", [P, 2, SET, P], F32, o2)
        assert _ <= nc.sbuf_usable_end and o + 2 * TILES * 2 * P * 2 <= nc.sbuf_usable_end, (o, _)
        acc, g = at("acc", [P, TILES, WIDE], F32, base0 + 60 * 1024)
        assert base0 + 60 * 1024 >= base0 + 32000 + TILES * P * 4 and g <= base0 + 2 * TILES * PARTS * 2 + SLOTS * TILES * P * 2
        rows_all, g = at("rows_all", [P, TILES, WIDE], F32, o)
        picked, g = at("picked", [P, WIDE], F32, g)
        edge_in, g = at("edge_in", [P, 3], I32, g)
        pick, g = at("pick", [P, 1], I32, g)
        keys, g = at("keys", [P, 2 + TILES], F32, g)
        gio, g = at("gio", [P, P], F32, g)
        shift, g = at("shift", [P, TILES], F32, g)
        one_hot, g = at("one_hot", [P, P], F32, g)
        dinv, g = at("dinv", [P, TILES], F32, g)
        assert g <= nc.sbuf_usable_end, g
        OT, _ = at("OT", [P, TILES, P], F32, base0)

        ps = ctx.enter_context(nc.psum_tensor("ps", [P, 8, 512], F32))
        ps16 = ps[:].rearrange("p b n -> p (b n)").bitcast(F16).rearrange("p (b n) -> p b n", b=8)

        def vec(ap):
            return ap.rearrange("(a b) -> a b", a=1)

        def spread(ap, n):
            return bass.AP(ap.tensor, 0, [[0, P], [1, n]])

        block = ctx.enter_context(nc.Block())

        def copy_turned(eng, copy, j, k, c, parity):
            e, tb = 2 + parity, (c // 2) % 2
            for g in range(SET):
                n = SET * c + g
                if n % 2 == parity:
                    eng.wait_ge(s(f"turned{e}"), k * 14 + n // 2 + 1)
                    if g < 2 and later(j, SLOTS):
                        eng.wait_ge(s(f"t_stored{tb}"), (k + c // SLOTS) * 16)
                    copy(t_stage[:, tb, g * SET:(g + 1) * SET, c % 2, :],
                         ps16[:, e, 0:SET * P].rearrange("p (i f) -> p i f", i=SET)).then_inc(s(f"t_copied{e}"), 1)

        def branch(eng, layers):
            eng.wait_ge(s("flag"), 1)
            found = eng.value_load(flag[0:1, 0:1], min_val=0, max_val=2 * P)
            with eng.If(found == 0):
                layers(False)
            with eng.Else():
                layers(True)

        def stages_stored(eng, ph):
            name = {1: "a_stored", 2: "t_stored"}.get(ph)
            if name:
                eng.wait_ge(s(name + "0"), 16 * (25 if ph == 1 else 13))
                eng.wait_ge(s(name + "1"), 16 * (24 if ph == 1 else 12))

        @block.sync
        def _(sp):
            for a, b in ((dst, dst_pad), (src, src_pad), (edge_weight.bitcast(I32), w_pad)):
                sp.dma_start(b[0:EDGES].rearrange("(a b) -> a b", a=15), a.rearrange("(a b) -> a b", a=15)).then_inc(s("pad_in"), 16)
            sp.wait_ge(s("pads"), 2)
            for k, b in ((1, dst_pad), (0, src_pad), (0, w_pad)):
                sp.dma_start(vec(b[EDGES:PADDED]), pad_rows[0:1, k, :]).then_inc(s("pad_in"), 16)
            sp.dma_start(X[:, 0:TILES - 1, :], x[0:(TILES - 1) * P].rearrange("(i p) f -> p i f", p=P)).then_inc(s("x_in"), 16)
            sp.wait_ge(s("x_zero"), 1)
            sp.dma_start(X[0:LAST, TILES - 1, :], x[(TILES - 1) * P:NODES]).then_inc(s("x_in"), 16)
            for to, of in ((w0g[:, 0:P], w0), (w0g[:, P:P + 1], wg0), (w3s[:], w3), (w_h[:, 0], wu[0:P]),
                           (wraw[:, 0], w1), (wraw[:, 1], wm[0:P]), (wraw[:, 2], wm[P:2 * P]), (wraw[:, 3], wu[P:2 * P]),
                           (b1s[:], spread(b1, P)), (bus[:], spread(bu, P)), (cols[:, 4:5], spread(bg0, 1)),
                           (cols[:, 0:1], bm.rearrange("(a b) -> a b", b=1)), (cols[:, 1:2], b3.rearrange("(a b) -> a b", b=1)),
                           (cols[:, 2:3], gamma.rearrange("(a b) -> a b", b=1)), (cols[:, 3:4], beta.rearrange("(a b) -> a b", b=1))):
                sp.dma_start(to, of).then_inc(s("weights_in"), 16)
            sp.wait_ge(s("x_zero"), 2)
            sp.dma_start(hrows[0:TILES - 1, :], hyper[0:(TILES - 1) * P].rearrange("(i p) -> i p", p=P)).then_inc(s("weights_in"), 16)
            sp.dma_start(hrows[TILES - 1:TILES, 0:LAST], vec(hyper[(TILES - 1) * P:NODES])).then_inc(s("weights_in"), 16)
            sp.wait_ge(s("pad_in"), 96)
            sp.dma_start(dst_run[:], bass.AP(dst_pad.tensor, 0, [[RUN, P], [1, RUN + 1]])).then_inc(s("dst_in"), 16)
            for k, b in enumerate((src_pad, dst_pad, w_pad)):
                sp.dma_start(table[:, k * P:(k + 1) * P], bass.AP(b.tensor, 0, [[ALIGN, ROWS], [1, P]])).then_inc(s("table_in"), 16)

            def layers(general):
                if general:
                    for ph in range(5):
                        general_sum(ph)
                    return
                def store_counts(j, b):
                    sp.wait_ge(s("evacuated"), (j + 1) * 16)
                    sp.dma_start(slab(a_dram, j), stage_a[:, b].rearrange("p i d -> p (i d)")).then_inc(s(f"a_stored{b}"), 16)

                pairs_loop(sp, lambda j, b, n: store_counts(j, b))
                sp.wait_ge(s("a_stored0"), 16 * 25)
                sp.wait_ge(s("a_stored1"), 16 * 24)

                for ph in (1, 2, 3, 4):
                    if ph == 1:
                        sp.wait_ge(s("added"), FOURS * TILES)
                    if ph == 4:
                        sp.wait_ge(s("t_stored0"), 16 * 13)
                        sp.wait_ge(s("t_stored1"), 16 * 12)

                    def step(j, k, c, ph=ph, source=at_dram if ph == 4 else a_dram):
                        q = c % SLOTS
                        if on(j):
                            if later(j, SLOTS):
                                sp.wait_ge(s(f"sum_done{ph}"), j - (SLOTS - 1))
                            elif ph > 1:
                                sp.wait_ge(s(f"sum_done{ph - 1}"), TILES)
                            sp.dma_start(a_tiles[:, q].rearrange("p i d -> p (i d)"), slab(source, j)).then_inc(s(f"a_in{q}"), 16)
                        if ph == 1 and on(j, SLOTS):
                            t = j - SLOTS
                            rows = at_dram.rearrange("i p n -> p i n")
                            if q % 2 or (isinstance(t, int) and t == TILES - 1):
                                b = (q // 2) % 2
                                for e in (2, 3):
                                    sp.wait_ge(s(f"t_copied{e}"), k * 14 + (7 * (c - SLOTS) + 7 + (1 if e == 2 else 0)) // 2)
                                if q % 2:
                                    to = rows[:, :, bass.ds((t - 1) * P, 2 * P)] if not isinstance(t, int) else rows[:, :, (t - 1) * P:(t + 1) * P]
                                    sp.dma_start(to, t_stage[:, b].rearrange("p i j d -> p i (j d)")).then_inc(s(f"t_stored{b}"), 16)
                                else:
                                    sp.dma_start(rows[:, :, t * P:(t + 1) * P], t_stage[:, b, :, 0, :]).then_inc(s(f"t_stored{b}"), 16)

                    tiles_loop(sp, step, SLOTS if ph == 1 else 0)

            def general_sum(ph):
                sp.wait_ge(s("g_rows_all"), ph + 1)
                sp.dma_start(h_dram.rearrange("(i p) f -> p i f", p=P), rows_all[:]).then_inc(s("g_table"), 16)
                with sp.Fori(0, CHUNKS) as c:
                    sp.wait_ge(s("g_free"), c + (ph * (CHUNKS + 1) + 1))
                    for a, b in enumerate((src_pad, dst_pad, w_pad)):
                        sp.dma_start(edge_in[:, a:a + 1], b[bass.ds(c * P, P)].rearrange("(a b) -> a b", b=1)).then_inc(s("g_in"), 16)

            branch(sp, layers)

            for g in range(6):
                sp.wait_ge(s("x_out"), 8 * (g + 1))
                sp.dma_start(out[g * 8 * P:(g + 1) * 8 * P].rearrange("(i p) f -> p i f", p=P), X[:, g * 8:(g + 1) * 8, :]).then_inc(s("stored"), 16)
            sp.wait_ge(s("x_out"), TILES)
            sp.dma_start(out[(TILES - 1) * P:NODES], X[0:LAST, TILES - 1, :]).then_inc(s("stored"), 16)
            sp.wait_ge(s("stored"), 16 * 7)

        @block.gpsimd
        def _(pool):
            g = nc.gpsimd
            g.memset(pad_rows[0:1, 0, :], 0).then_inc(s("pads"), 1)
            g.memset(pad_rows[0:1, 1, :], NO_NODE).then_inc(s("pads"), 1)
            g.memset(X[:, TILES - 1, :], 0.0).then_inc(s("x_zero"), 1)
            g.memset(hrows[:], 0.0).then_inc(s("x_zero"), 1)
            g.iota(diff[:], pattern=[[1, P]], base=0, channel_multiplier=-1).then_inc(s("iotas"), 1)
            g.iota(basei[:], pattern=[[-TILES * WD * P, GROUPS]], base=0, channel_multiplier=-TILES * WD).then_inc(s("iotas"), 1)
            g.iota(io_b[:], pattern=[[1, P]], base=0, channel_multiplier=0, allow_small_or_imprecise_dtypes=True).then_inc(s("iotas"), 1)
            g.iota(iota_r[:], pattern=[[1, P], [0, HOT]], base=0, channel_multiplier=0, allow_small_or_imprecise_dtypes=True).then_inc(s("iotas"), 1)
            g.iota(iota_c[:], pattern=[[1, WCOLS], [0, HOT]], base=0, channel_multiplier=0, allow_small_or_imprecise_dtypes=True).then_inc(s("iotas"), 1)
            pool.wait_ge(s("first_ready"), 1)
            pool.wait_ge(s("table_in"), 48)
            for n in range(GROUPS):
                g.indirect_dma_start(out=rec[:, n, :], out_offset=None, in_=table,
                                     in_offset=IndirectOffsetOnAxis(ap=first[:, n:n + 1], axis=0)).then_inc(s("rec_in"), 16)

            def layers(general):
                if not general:
                    return
                pool.wait_ge(s("meta"), GROUPS // 5)
                g.iota(gio[:], pattern=[[1, P]], base=0, channel_multiplier=0, allow_small_or_imprecise_dtypes=True)
                g.iota(shift[:], pattern=[[-P, TILES]], base=0, channel_multiplier=0, allow_small_or_imprecise_dtypes=True).then_inc(s("g_iotas"), 1)
                for ph in range(5):
                    pool.wait_ge(s("g_table"), 16 * (ph + 1))
                    with pool.Fori(0, CHUNKS):
                        pool.wait_ge(s("g_pick"), 1)
                        pool.sem_clear(s("g_pick"))
                        g.indirect_dma_start(out=picked[:], out_offset=None, in_=h_dram,
                                             in_offset=IndirectOffsetOnAxis(ap=pick[:, 0:1], axis=0)).then_inc(s(f"g_picked{ph}"), 16)

            branch(pool, layers)

        @block.tensor
        def _(pe):
            mm, tr = nc.tensor.matmul, nc.tensor.transpose
            pe.wait_ge(s("weights_in"), 16 * 17)
            pe.wait_ge(s("consts"), 1)
            tr(ps[:, 0, 0:P], wraw[:, 0], ident[:])
            tr(ps[:, 0, P:2 * P], wraw[:, 1], ident[:])
            tr(ps[:, 0, 3 * P:4 * P], hrows[:], ident[:])
            tr(ps[:, 0, 2 * P:3 * P], wraw[:, 2], ident[:]).then_inc(s("w_ps"), 1)
            pe.wait_ge(s("w_t"), 1)
            mm(ps[:, 1, 0:P], wraw[:, 4], wraw[:, 3], start=True, stop=True)
            mm(ps[:, 1, P:2 * P], wraw[:, 5], wraw[:, 3], start=True, stop=True)
            mm(ps[:, 1, 2 * P:3 * P], wraw[:, 6], wraw[:, 3], start=True, stop=True).then_inc(s("w_ps"), 1)
            pe.wait_ge(s("hot_samples"), 1)
            for f in range(SAMPLES):
                last = mm(ps[:, 2, 0:GROUPS], hot_b[:, f, :], hot_g[:, f, :], start=f == 0, stop=f == SAMPLES - 1)
            last.then_inc(s("hist_ps"), 1)
            pe.wait_ge(s("hist"), 1)
            mm(ps[:, 3, 0:GROUPS], before[:], hist[:], start=True, stop=True)
            mm(ps[:, 3, 32:32 + GROUPS], ones[:], hist[:], start=True, stop=True).then_inc(s("hist_ps"), 1)
            pe.wait_ge(s("bad"), 1)
            mm(ps[:, 3, 64:65], ones[:], bad[:, 3:4], start=True, stop=True).then_inc(s("bad_ps"), 1)

            def first_step(j, k, c):
                if on(j):
                    pe.wait_ge(s("h0_row"), j + 1)
                    if later(j, 2):
                        pe.wait_ge(s("h0_copied"), j - 1)
                    tr(ps[:, 4 + c % 2, 0:P], hs0[:, c % SLOTS], ident[:]).then_inc(s("h0_turned"), 1)
                if on(j, 1):
                    t, d = j - 1, c - 1
                    pe.wait_ge(s("h0_copied"), t + 1)
                    if later(t, 2):
                        pe.wait_ge(s("h0_done"), t - 1)
                    mm(ps[:, 6 + d % 2, 0:P + 1], hts0[:, d % SLOTS], w0g[:], start=True, stop=True).then_inc(s("h0_mm"), 1)

            tiles_loop(pe, first_step, 1)

            with pe.Fori(0, GROUPS // 5) as k:
                for u in range(5):
                    n = k * 5 + u
                    pe.wait_ge(s("pre"), n + 1)
                    for a in range(3):
                        last = tr(ps[:, u, a * P:(a + 1) * P], pre[:, u, a], ident[:])
                    last.then_inc(s("turned"), 1)

            def general_sum(ph):
                with pe.Fori(0, CHUNKS) as c:
                    with pe.Fori(0, TILES) as j:
                        pe.wait_ge(s("g_hot"), (c + ph * CHUNKS) * TILES + j + 1)
                        mm(ps[:, 0, 0:WIDE], one_hot[:], picked[:], start=True, stop=True).then_inc(s("g_mm"), 1)

            def layers(general):
                def turn_weights(t, b, g):
                    n, e = t * FOURS + g, (b + g) % 2
                    if not (isinstance(t, int) and t * FOURS + g < 2):
                        pe.wait_ge(s("wt_copied"), n - 1)
                    for i in range(4 * g, min(4 * g + 4, TILES)):
                        last = tr(ps[:, 4 + e, (i % 4) * P:(i % 4 + 1) * P], stage_w[:, b, i], ident[:])
                    last.then_inc(s("wt_turned"), 1)

                def sum_four(t, b, g):
                    n, e = t * FOURS + g, (b + g) % 2
                    pe.wait_ge(s("wt_copied"), n + 1)
                    if not (isinstance(t, int) and t * FOURS + g < 2):
                        pe.wait_ge(s("added"), n - 1)
                    for i in range(4 * g, min(4 * g + 4, TILES)):
                        last = mm(ps[:, 6 + e, (i % 4) * P:(i % 4 + 1) * P], wt[:, e, i % 4], row(H0, t), start=True, stop=True)
                    last.then_inc(s("four_done"), 1)

                def build(j, b, behind):
                    for h in range(TILE_HOTS):
                        hot = j * TILE_HOTS + h
                        pe.wait_ge(s("hot_ready"), hot + 1)
                        for half in range(2):
                            if not (isinstance(j, int) and j == 0 and h == 0):
                                pe.wait_ge(s("evacuated"), hot * 2 + half - 1)
                            for v in range(HALF):
                                win = half * HALF + v
                                bank, place_ = half * 2 + v // 2, (v % 2) * WCOLS
                                both = ps[:, bank, 0:4 * WCOLS].rearrange("p (a n) -> p a n", a=2)[:, :, place_:place_ + WCOLS]
                                weighted = ps[:, bank, 2 * WCOLS + place_:3 * WCOLS + place_]
                                rows_ = hot_r[:, h % 2, :, win]
                                mm(weighted, rows_, hot_c[:, h % 2, 2, :, win], start=True, stop=False)
                                mm(weighted, rows_, hot_c[:, h % 2, 3, :, win], start=False, stop=True)
                                last = mm(both, rows_, hot_c[:, h % 2, 0:2, :, win], start=False, stop=True, skip_group_check=True)
                            last.then_inc(s("unit_done"), 1)
                        if behind:
                            if h == 0:
                                pe.wait_ge(s("evacuated"), j * 16)
                            behind_step(j - 1, 1 - b, h)

                def behind_step(t, b, h):
                    for g in turned_at(h):
                        turn_weights(t, b, g)
                    for g in summed_at(h):
                        sum_four(t, b, g)

                if general:
                    general_sum(0)
                else:
                    pairs_loop(pe, lambda j, b, n: build(j, b, not isinstance(j, int) or j > 0))
                    pe.wait_ge(s("evacuated"), TILES * 16)
                    for h in range(TILE_HOTS):
                        behind_step(TILES - 1, 0, h)

                for ph in (1, 2, 3, 4):
                    moving = Hb if ph == 4 else Ha

                    def step(j, k, c, ph=ph, moving=moving):
                        q = c % SLOTS
                        if on(j) and not general:
                            pe.wait_ge(s(f"a_in{q}"), (k + (tiles_before(ph, q) + c // SLOTS + 1)) * 16)
                            if later(j, 2):
                                pe.wait_ge(s(f"low_ready{ph}"), j - 1)
                                pe.wait_ge(s(f"agg_ready{ph}"), j - 1)
                            for i in range(TILES):
                                if ph == 1 and i % SET == 0:
                                    turn(j, k, c, i // SET)
                                last = mm(ps[:, c % 2, 0:PARTS], a_tiles[:, q, i], moving[:, i], start=i == 0, stop=i == TILES - 1)
                            last.then_inc(s(f"sum_done{ph}"), 1)
                        if ph != 3 and on(j, 1):
                            t, d = j - 1, c - 1
                            pe.wait_ge(s(f"agg_ready{ph}"), t + 1)
                            if later(t, 2):
                                pe.wait_ge(s(f"aggt_ready{ph}"), t - 1)
                            if ph == 2:
                                pe.wait_ge(s("hrow_ready"), t + 1)
                                tr(ps[:, 4 + d % 2, P:2 * P], hrow[:, d % SLOTS], ident[:])
                            tr(ps[:, 4 + d % 2, 0:P], agg[:, d % SLOTS], ident[:]).then_inc(s(f"t_done{ph}"), 1)
                        if ph != 3 and on(j, 2):
                            t, d = j - 2, c - 2
                            pe.wait_ge(s(f"aggt_ready{ph}"), t + 1)
                            if later(t, 2):
                                pe.wait_ge(s(f"upd_done{ph}"), t - 1)
                            o = ps[:, 6 + d % 2, :]
                            if ph == 1:
                                last = mm(o[:, 0:P], aggt[:, d % SLOTS, 0], w1t[:], start=True, stop=True)
                            elif ph == 2:
                                mm(o[:, 0:P], aggt[:, d % SLOTS, 0], w_s[:], start=True, stop=True)
                                last = mm(o[:, 0:2 * P], aggt[:, d % SLOTS, 1], w_h[:].rearrange("p a f -> p (a f)"), start=False, stop=True, skip_group_check=True)
                            else:
                                last = mm(o[:, 0:P], w3s[:], aggt[:, d % SLOTS, 0], start=True, stop=True)
                            last.then_inc(s(f"mm_done{ph}"), 1)

                    def turn(j, k, c, g):
                        n = SET * c + g
                        e = 2 + n % 2
                        if not (isinstance(j, int) and n < 2):
                            pe.wait_ge(s(f"t_copied{e}"), k * 14 + n // 2)
                        for i in range(SET):
                            last = tr(ps16[:, e, i * P:(i + 1) * P], a_tiles[:, c % SLOTS, g * SET + i], ident16[:])
                        last.then_inc(s(f"turned{e}"), 1)

                    if general:
                        general_sum(ph)
                    else:
                        pe.wait_ge(s(f"h_ready{ph}"), SET if ph < 4 else TILES)
                    if not (general and ph == 3):
                        tiles_loop(pe, step, 2)

            branch(pe, layers)

            def last_step(j, k, c):
                if on(j):
                    pe.wait_ge(s("y_ready"), j + 1)
                    if later(j, 2):
                        pe.wait_ge(s("x_out"), j - 1)
                    tr(ps[:, 4 + c % 2, 0:P], hrow[:, c % SLOTS], ident[:]).then_inc(s("y_turned"), 1)

            tiles_loop(pe, last_step, 0)

        @block.vector
        def _(dve):
            v = nc.vector
            dve.wait_ge(s("iotas"), 5)
            v.tensor_scalar(ident[:], diff[:], 0, None, ALU.is_equal)
            v.tensor_scalar(ident16[:], diff[:], 0, None, ALU.is_equal)
            v.tensor_scalar(before[:], diff[:], 0, None, ALU.is_gt)
            v.tensor_copy(basef[:], basei[:])
            v.memset(ones[:], 1.0).then_inc(s("consts"), 1)
            dve.wait_ge(s("consts"), 1)
            dve.wait_ge(s("weights_in"), 16 * 17)
            v.tensor_scalar(wraw[:, 6], ones[:], cols[:, 0:1], None, ALU.mult)
            dve.wait_ge(s("w_ps"), 1)
            v.tensor_copy(w1t[:], ps[:, 0, 0:P])
            v.tensor_copy(hyp[:], ps[:, 0, 3 * P:3 * P + TILES])
            v.tensor_copy(wraw[:, 4:6].rearrange("p a f -> p (a f)"), ps[:, 0, P:3 * P]).then_inc(s("w_t"), 1)
            dve.wait_ge(s("w_ps"), 2)
            v.tensor_copy(w_s[:], ps[:, 1, 0:P])
            v.tensor_copy(w_h[:, 1], ps[:, 1, P:2 * P])
            v.tensor_copy(bmu[:], ps[:, 1, 2 * P:3 * P])

            ch = Chain(dve, s("dve"))
            dve.wait_ge(s("dst_in"), 16)
            v.tensor_tensor(viol[:], dst_run[:, 0:RUN], dst_run[:, 1:RUN + 1], ALU.is_gt)
            runs = dst_run[:, 0:RUN].rearrange("p (n a) -> p n a", a=ALIGN)[:, :, 0]
            v.tensor_scalar(smp[:, 0], runs, 1, P - 1, ALU.logical_shift_right, ALU.bitwise_and)
            ch(v.tensor_scalar(smp[:, 1], runs, 8, None, ALU.logical_shift_right))
            ch(v.tensor_copy(smpf[:], smp[:]))
            v.tensor_tensor(hot_g[:], io_b[:, 0:GROUPS].unsqueeze(1).to_broadcast([P, SAMPLES, GROUPS]),
                            smpf[:, 1].unsqueeze(2).to_broadcast([P, SAMPLES, GROUPS]), ALU.is_equal)
            v.tensor_tensor(hot_b[:], io_b[:].unsqueeze(1).to_broadcast([P, SAMPLES, P]),
                            smpf[:, 0].unsqueeze(2).to_broadcast([P, SAMPLES, P]), ALU.is_equal).then_inc(s("hot_samples"), 1)
            v.tensor_reduce(bad[:, 0:1], viol[:], AX.X, ALU.max)
            dve.wait_ge(s("hist_ps"), 1)
            v.tensor_copy(hist[:], ps[:, 2, 0:GROUPS]).then_inc(s("hist"), 1)
            dve.wait_ge(s("hist_ps"), 2)
            dve.wait_ge(s("hist"), 1)
            v.tensor_reduce(bad[:, 1:2], hist[:], AX.X, ALU.max)
            ch(v.tensor_copy(tot[:, 0], ps[:, 3, 32:32 + GROUPS]))
            ch(v.tensor_tensor_scan(tot[:, 1], ones[:, 0:GROUPS], tot[:, 0], 0.0, ALU.mult, ALU.add))
            ch(v.tensor_tensor(tot[:, 2], tot[:, 1], tot[:, 0], ALU.subtract))
            ch(v.tensor_tensor(tot[:, 1], tot[:, 2], ps[:, 3, 0:GROUPS], ALU.add))
            v.tensor_scalar(first[:], tot[:, 1], -1.0, 0.0, ALU.add, ALU.max).then_inc(s("first_ready"), 1)
            ch(v.tensor_scalar(bad[:, 2:3], bad[:, 1:2], float(FITS), None, ALU.is_gt))
            v.tensor_tensor(bad[:, 3:4], bad[:, 2:3], bad[:, 0:1], ALU.add).then_inc(s("bad"), 1)
            dve.wait_ge(s("bad_ps"), 1)
            v.tensor_copy(flag[:], ps[:, 3, 64:65]).then_inc(s("flag"), 1)

            def norm(ph):
                c = Chain(dve, s(f"norm{ph}"))
                half = lambda a: stats[:, :, a]
                v.tensor_tensor(t49[:, 0], half(1), half(4), ALU.add)
                v.tensor_tensor(t49[:, 1], half(1), half(4), ALU.subtract)
                c(v.tensor_tensor(t49[:, 2], half(2), half(5), ALU.add))
                v.tensor_tensor(t49[:, 1], t49[:, 1], t49[:, 1], ALU.mult)
                c(v.tensor_scalar(t49[:, 2], t49[:, 2], 1.0 / P, EPS, ALU.mult, ALU.add))
                v.scalar_tensor_tensor(t49[:, 1], t49[:, 1], 0.25, t49[:, 2], ALU.mult, ALU.add).then_inc(s(f"var{ph}"), 1)
                dve.wait_ge(s(f"std{ph}"), 1)
                c(v.reciprocal(rstd[:], t49[:, 1]))
                v.scalar_tensor_tensor(nmr[:], t49[:, 0], -0.5, rstd[:], ALU.mult, ALU.mult).then_inc(s(f"normed{ph}"), 1)

            dve.wait_ge(s("x_in"), 32)
            for j in range(TILES):
                last = v.bn_stats(stats[:, j], X[:, j])
            last.then_inc(s("stats0"), 1)
            dve.wait_ge(s("stats0"), 1)
            norm(0)

            def first_step(j, k, c):
                if on(j):
                    dve.wait_ge(s("h0_turned"), j + 1)
                    if later(j, SLOTS):
                        dve.wait_ge(s("h0_mm"), j - (SLOTS - 1))
                    v.tensor_copy(hts0[:, c % SLOTS], ps[:, 4 + c % 2, 0:P]).then_inc(s("h0_copied"), 1)

            tiles_loop(dve, first_step, 0)

            dve.wait_ge(s("rec_in"), 16 * GROUPS)
            dve.wait_ge(s("h0_done"), TILES)
            with dve.Fori(0, GROUPS // 5) as k:
                for u in range(5):
                    n = k * 5 + u
                    c = Chain(dve, s("dve_pre"), n * 3)
                    field = lambda a: rec[:, bass.ds(n, 1), a * P:(a + 1) * P].rearrange("p a f -> p (a f)")
                    v.tensor_scalar(ri[:, u, 0], field(0), P - 1, None, ALU.bitwise_and)
                    c(v.tensor_scalar(ri[:, u, 1], field(0), 7, None, ALU.logical_shift_right))
                    v.tensor_copy(pre[:, u, 0], ri[:, u, 0])
                    v.tensor_copy(pre[:, u, 2], field(2).bitcast(F32))
                    c(v.scalar_tensor_tensor(pre[:, u, 1], field(1), float(TILES), ri[:, u, 1], ALU.mult, ALU.add))
                    c(v.tensor_scalar(pre[:, u, 1], pre[:, u, 1], basef[:, bass.ds(n, 1)], -1.0, ALU.add, ALU.max))
                    v.tensor_scalar(pre[:, u, 1], pre[:, u, 1], 255.0, None, ALU.min).then_inc(s("pre"), 1)
                for u in range(5):
                    n = k * 5 + u
                    c = Chain(dve, s("dve_meta"), n * 4)
                    part = lambda a: meta[:, a, bass.ds(n * P, P)]
                    dve.wait_ge(s("turned"), n + 1)
                    v.tensor_copy(part(0), ps[:, u, 0:P])
                    v.tensor_copy(part(1), ps[:, u, P:2 * P])
                    c(v.tensor_copy(part(2), ps[:, u, 2 * P:3 * P]))
                    c(v.tensor_tensor(wres[:, u, 0], ps[:, u, 2 * P:3 * P], part(2), ALU.subtract))
                    c(v.tensor_copy(part(3), wres[:, u, 0]))
                    c(v.tensor_tensor(wres[:, u, 1], wres[:, u, 0], part(3), ALU.subtract))
                    last = v.tensor_copy(part(4), wres[:, u, 1])
                last.then_inc(s("meta"), 1)
            dve.wait_ge(s("meta"), GROUPS // 5)

            def degrees(c):
                c(v.tensor_copy(indeg[:], extra[:, :, 0]))
                v.tensor_scalar(t49[:, 0], indeg[:], 1.0, None, ALU.max)
                c(v.tensor_scalar(t49[:, 1], indeg[:], 0.0, None, ALU.is_gt))
                c(v.reciprocal(t49[:, 2], t49[:, 0]))
                c(v.tensor_tensor(binv[:], t49[:, 2], t49[:, 1], ALU.mult))

            def general_sum(ph):
                to, of = (0, 1) if ph in (0, 4) else (1, 0)
                v.memset(acc[:], 0.0).then_inc(s("g_free"), 1)
                dve.wait_ge(s("g_free"), ph * (CHUNKS + 1) + 1)
                with dve.Fori(0, CHUNKS) as n:
                    c = Chain(dve, s("g_chain"), (n + ph * CHUNKS) * 2)
                    dve.wait_ge(s("g_in"), (n + (ph * CHUNKS + 1)) * 48)
                    if ph == 0:
                        v.tensor_copy(keys[:, 1:2], edge_in[:, 2:3].bitcast(F32))
                    else:
                        v.tensor_scalar(keys[:, 1:2], edge_in[:, 1:2], float(NODES), None, ALU.is_lt)
                    c(v.tensor_copy(keys[:, 0:1], edge_in[:, to:to + 1]))
                    v.tensor_scalar(pick[:], edge_in[:, of:of + 1], float(NODES - 1), None, ALU.min).then_inc(s("g_pick"), 1)
                    c(v.tensor_scalar(keys[:, 2:], shift[:], keys[:, 0:1], None, ALU.add))
                    dve.wait_ge(s(f"g_picked{ph}"), n * 16 + 16)
                    v.memset(small[:, 0, 7:8], 0.0).then_inc(s("g_free"), 1)
                    with dve.Fori(0, TILES) as j:
                        v.tensor_scalar(one_hot[:], gio[:], keys[:, bass.ds(j + 2, 1)], keys[:, 1:2], ALU.is_equal, ALU.mult).then_inc(s("g_hot"), 1)
                        dve.wait_ge(s("g_mm"), (n + ph * CHUNKS) * TILES + j + 1)
                        v.tensor_tensor(row(acc, j), row(acc, j), ps[:, 0, 0:WIDE], ALU.add).then_inc(s("g_add"), 1)
                        dve.wait_ge(s("g_add"), (n + ph * CHUNKS) * TILES + j + 1)

            def layers(general):
                def hots(j, h):
                    b = h % 2
                    hot = j * TILE_HOTS + h
                    if not (isinstance(j, int) and j == 0 and h < 2):
                        dve.wait_ge(s("unit_done"), hot * 2 - 2)
                    of = lambda a: meta[:, a, bass.ds(hot * HOT, HOT)] if not isinstance(hot, int) else meta[:, a, hot * HOT:(hot + 1) * HOT]
                    v.tensor_tensor(hot_c[:, b, 0], iota_c[:], of(1).unsqueeze(1).to_broadcast([P, WCOLS, HOT]), ALU.is_equal).then_inc(s("hot_codes"), 1)
                    v.tensor_tensor(hot_r[:, b], iota_r[:], of(0).unsqueeze(1).to_broadcast([P, P, HOT]), ALU.is_equal)
                    dve.wait_ge(s("hot_codes"), hot + 1)
                    w = meta[:, 2:5, bass.ds(hot * HOT, HOT)] if not isinstance(hot, int) else meta[:, 2:5, hot * HOT:(hot + 1) * HOT]
                    v.tensor_tensor(hot_c[:, b, 1:4], hot_c[:, b, 0].unsqueeze(1).to_broadcast([P, 3, WCOLS, HOT]),
                                    w.unsqueeze(2).to_broadcast([P, 3, WCOLS, HOT]), ALU.mult).then_inc(s("hot_ready"), 1)

                def add_four(t, b, g):
                    n, e = t * FOURS + g, (b + g) % 2
                    lo, hi = 4 * g, min(4 * g + 4, TILES)
                    dve.wait_ge(s("four_done"), n + 1)
                    if not (isinstance(t, int) and t == 0):
                        dve.wait_ge(s("added"), n - (FOURS - 1))
                    xs = X[:, lo:hi].rearrange("p i f -> p (i f)")
                    v.tensor_tensor(xs, xs, ps[:, 6 + e, 0:(hi - lo) * P], ALU.add).then_inc(s("added"), 1)

                def build(j, b, n):
                    for h in range(TILE_HOTS):
                        hots(j, h)
                        t, tb, hh = (j - 1, 1 - b, h - 2) if h >= 2 else (j - 2, b, h + TILE_HOTS - 2)
                        if not isinstance(t, int) or t >= 0:
                            for g in summed_at(hh):
                                add_four(t, tb, g)

                if general:
                    dve.wait_ge(s("g_iotas"), 1)
                    v.memset(rows_all[:], 0.0).then_inc(s("g_zero"), 1)
                    dve.wait_ge(s("g_zero"), 1)
                    v.tensor_copy(rows_all[:, :, 0:P], H0[:]).then_inc(s("g_rows_all"), 1)
                    general_sum(0)
                    v.tensor_tensor(X[:], X[:], acc[:, :, 0:P], ALU.add).then_inc(s("g_x"), 1)
                    dve.wait_ge(s("g_x"), 1)
                else:
                    pairs_loop(dve, build)
                    for h in range(TILE_HOTS - 2, TILE_HOTS):
                        for g in summed_at(h):
                            add_four(TILES - 2, 1, g)
                    for g in range(FOURS):
                        add_four(TILES - 1, 0, g)
                    dve.wait_ge(s("added"), FOURS * TILES)
                for j in range(TILES):
                    v.bn_stats(stats[:, j], X[:, j])

                def split(ph):
                    stages_stored(dve, ph)
                    for c in range(SET):
                        dve.wait_ge(s(f"split_h{ph}"), c + 1)
                        to = Ha[:, c * SET:(c + 1) * SET, 0:P]
                        v.tensor_copy(to, hbig[:, c % 2]).then_inc(s(f"split_hi{ph}"), 1)
                        dve.wait_ge(s(f"split_hi{ph}"), c + 1)
                        if c >= 2:
                            dve.wait_ge(s(f"h_ready{ph}"), c - 1)
                        v.tensor_tensor(dbig[:, c % 2], hbig[:, c % 2], to, ALU.subtract).then_inc(s(f"split_d{ph}"), 1)

                for ph in (1, 2, 3, 4):
                    if ph < 4:
                        v.memset(t49[:], 0.0).then_inc(s(f"stats{ph}"), 1)
                        dve.wait_ge(s(f"stats{ph}"), 1)
                        norm(ph)
                        if general:
                            if ph == 1:
                                v.memset(rows_all[:, :, P:P + 1], 1.0).then_inc(s("g_ones"), 1)
                            dve.wait_ge(s("g_h"), TILES * ph)
                            dve.wait_ge(s("g_ones"), 1)
                            v.memset(small[:, 0, 6:7], 0.0).then_inc(s("g_rows_all"), 1)
                        else:
                            if ph == 1:
                                v.memset(Ha[:, :, 2 * P:2 * P + 1], 1.0)
                                v.memset(Ha[:, :, 2 * P + 1:PARTS], 0.0)
                            split(ph)
                    if general:
                        general_sum(ph)
                        e = Chain(dve, s(f"g_after{ph}"))
                        e(v.tensor_copy(extra[:], acc[:, :, P:WIDE]))
                        if ph == 1:
                            degrees(e)
                        if ph == 3:
                            v.tensor_copy(rows_all[:, :, P], hyp[:])
                            v.tensor_tensor(rows_all[:, :, 0:P], acc[:, :, 0:P], binv[:].unsqueeze(2).to_broadcast([P, TILES, P]), ALU.mult).then_inc(s("g_rows_all"), 1)
                            continue
                        if ph == 4:
                            e(v.tensor_scalar(t49[:, 0], extra[:, :, 0], 0.0, None, ALU.is_le))
                            e(v.tensor_tensor(t49[:, 0], t49[:, 0], extra[:, :, 0], ALU.max))
                            e(v.reciprocal(t49[:, 1], t49[:, 0]))
                            e(v.tensor_scalar(t49[:, 0], extra[:, :, 0], 0.0, None, ALU.is_gt))
                            e(v.tensor_tensor(dinv[:], t49[:, 0], t49[:, 1], ALU.mult))

                    def step(j, k, c, ph=ph):
                        q = c % SLOTS
                        if general and on(j):
                            if later(j, SLOTS):
                                dve.wait_ge(s(f"t_done{ph}"), j - (SLOTS - 1))
                            mine = acc[:, j, 0:P] if isinstance(j, int) else acc[:, bass.ds(j, 1), 0:P].rearrange("p a f -> p (a f)")
                            if ph == 4:
                                over = dinv[:, j:j + 1] if isinstance(j, int) else dinv[:, bass.ds(j, 1)]
                                v.tensor_scalar(agg[:, q], mine, over, None, ALU.mult).then_inc(s("agg_ready4"), 1)
                            else:
                                v.tensor_copy(agg[:, q], mine).then_inc(s(f"agg_ready{ph}"), 1)
                        if on(j) and not general:
                            if ph == 1:
                                copy_turned(dve, v.tensor_copy, j, k, c, 0)
                            dve.wait_ge(s(f"low_ready{ph}"), j + 1)
                            if ph != 3 and later(j, SLOTS):
                                dve.wait_ge(s(f"t_done{ph}"), j - (SLOTS - 1))
                            whole = ps[:, c % 2, 0:P]
                            if ph in (1, 2):
                                v.tensor_tensor(agg[:, q], whole, low[:, q], ALU.add).then_inc(s(f"agg_ready{ph}"), 1)
                            elif ph == 3:
                                v.tensor_tensor(agg[:, q], whole, low[:, q], ALU.add).then_inc(s(f"agg_ready{ph}"), 1)
                                dve.wait_ge(s(f"agg_ready{ph}"), j + 1)
                                e = Chain(dve, s("dve_e"), j * 2)
                                over = binv[:, j:j + 1] if isinstance(j, int) else binv[:, bass.ds(j, 1)]
                                e(v.tensor_scalar(upd[:, q, 0], agg[:, q], over, None, ALU.mult))
                                hi = Hb[:, j, 0:P] if isinstance(j, int) else Hb[:, bass.ds(j, 1), 0:P].rearrange("p a f -> p (a f)")
                                e(v.tensor_copy(hi, upd[:, q, 0]))
                                if later(j, SLOTS):
                                    dve.wait_ge(s("h_ready4"), j - (SLOTS - 1))
                                v.tensor_tensor(upd[:, q, 1], upd[:, q, 0], hi, ALU.subtract).then_inc(s("e_rest"), 1)
                            else:
                                m = small[:, q]
                                e = Chain(dve, s("dve_d"), j * 4)
                                ex = lambda a: extra[:, j, a:a + 1] if isinstance(j, int) else extra[:, bass.ds(j, 1), a:a + 1].rearrange("p a f -> p (a f)")
                                v.tensor_tensor(upd[:, q, 0], whole, low[:, q], ALU.add)
                                e(v.scalar_tensor_tensor(m[:, 0:1], ex(1), 1.0 / LOW, ex(0), ALU.mult, ALU.add))
                                v.tensor_scalar(m[:, 4:5], m[:, 0:1], 0.0, None, ALU.is_gt)
                                e(v.tensor_scalar(m[:, 1:2], m[:, 0:1], 0.0, None, ALU.is_le))
                                e(v.tensor_tensor(m[:, 2:3], m[:, 0:1], m[:, 1:2], ALU.max))
                                e(v.reciprocal(m[:, 3:4], m[:, 2:3]))
                                v.tensor_scalar(agg[:, q], upd[:, q, 0], m[:, 3:4], m[:, 4:5], ALU.mult, ALU.mult).then_inc(s(f"agg_ready{ph}"), 1)
                        if ph in (1, 2) and on(j, 2):
                            t, d = j - 2, c - 2
                            o = ps[:, 6 + d % 2, :]
                            dve.wait_ge(s(f"mm_done{ph}"), t + 1)
                            if ph == 1:
                                e = Chain(dve, s("dve_u1"), t)
                                v.tensor_tensor(row(X, t), row(X, t), o[:, 0:P], ALU.add).then_inc(s("upd_done1"), 1)
                                dve.wait_ge(s("upd_done1"), t + 1)
                                e(v.tensor_tensor(row(X, t), row(X, t), b1s[:], ALU.add))
                            else:
                                e = Chain(dve, s("dve_u2"), t * 3)
                                deg = indeg[:, t:t + 1] if isinstance(t, int) else indeg[:, bass.ds(t, 1)]
                                e(v.tensor_tensor(upd[:, d % SLOTS, 0], o[:, P:2 * P], bmu[:], ALU.add))
                                v.scalar_tensor_tensor(upd[:, d % SLOTS, 1], upd[:, d % SLOTS, 0], deg, o[:, 0:P], ALU.mult, ALU.add).then_inc(s("upd_done2"), 1)
                                dve.wait_ge(s("upd_done2"), t + 1)
                                e(v.tensor_tensor(row(X, t), row(X, t), upd[:, d % SLOTS, 1], ALU.add))
                                e(v.tensor_tensor(row(X, t), row(X, t), bus[:], ALU.add))
                            v.bn_stats(row(stats, t), row(X, t))

                    tiles_loop(dve, step, 2)
                    if ph == 1 and not general:
                        c1 = Chain(dve, s("dve_b"))
                        degrees(c1)
                        c1(v.tensor_copy(Hb[:, :, 2 * P], hyp[:]))
                        c1(v.tensor_tensor(t49[:, 0], hyp[:], Hb[:, :, 2 * P], ALU.subtract))
                        c1(v.tensor_scalar(Hb[:, :, 2 * P + 1], t49[:, 0], LOW, None, ALU.mult))

            branch(dve, layers)

            dve.wait_ge(s("upd_done4"), TILES)
            flat = OT[:].rearrange("p i n -> p (i n)")
            lots = [(a, min(a + 512, NODES)) for a in range(0, NODES, 512)]
            for n, (a, z) in enumerate(lots):
                last = v.bn_stats(stats[:, n], flat[:, a:z])
            c2 = Chain(dve, s("dve_f"))
            c2(last)
            c2(v.bn_aggr(fin[:, 0:2], stats[:, 0:len(lots)].rearrange("p n s -> p (n s)")))
            v.tensor_scalar(fin[:, 2:3], fin[:, 1:2], EPS, None, ALU.add).then_inc(s("bvar"), 1)
            dve.wait_ge(s("bstd"), 1)
            c2(v.reciprocal(fin[:, 4:5], fin[:, 3:4]))
            c2(v.tensor_tensor(fin[:, 5:6], fin[:, 4:5], cols[:, 2:3], ALU.mult))
            c2(v.tensor_tensor(fin[:, 6:7], fin[:, 5:6], fin[:, 0:1], ALU.mult))
            v.tensor_tensor(fin[:, 7:8], cols[:, 3:4], fin[:, 6:7], ALU.subtract).then_inc(s("batch"), 1)

            def last_step(j, k, c):
                if on(j):
                    dve.wait_ge(s("y_turned"), j + 1)
                    v.tensor_tensor(row(X, j), row(X, j), ps[:, 4 + c % 2, 0:P], ALU.add).then_inc(s("x_out"), 1)

            tiles_loop(dve, last_step, 0)

        @block.scalar
        def _(act):
            a = nc.scalar

            def std(ph):
                act.wait_ge(s(f"var{ph}"), 1)
                a.activation(t49[:, 1], t49[:, 1], ACT.Sqrt).then_inc(s(f"std{ph}"), 1)
                act.wait_ge(s(f"normed{ph}"), 1)

            def relu_row(to, j):
                col = lambda t: t[:, j:j + 1] if isinstance(j, int) else t[:, bass.ds(j, 1)]
                return a.activation(to, row(X, j), ACT.Relu, bias=col(nmr), scale=col(rstd))

            std(0)

            def first_step(j, k, c):
                if on(j):
                    if later(j, SLOTS):
                        act.wait_ge(s("h0_turned"), j - (SLOTS - 1))
                    relu_row(hs0[:, c % SLOTS], j).then_inc(s("h0_row"), 1)
                if on(j, 2):
                    t, d = j - 2, c - 2
                    act.wait_ge(s("h0_mm"), t + 1)
                    o = ps[:, 6 + d % 2, :]
                    a.activation(small[:, d % SLOTS, 0:1], o[:, P:P + 1], ACT.Sigmoid, bias=cols[:, 4:5]).then_inc(s("gated"), 1)
                    act.wait_ge(s("gated"), t + 1)
                    a.activation(row(H0, t), o[:, 0:P], ACT.Copy, scale=small[:, d % SLOTS, 0:1]).then_inc(s("h0_done"), 1)

            tiles_loop(act, first_step, 2)

            def layers(general):
                def copy_weights(t, b, h):
                    for g in turned_at(h):
                        n, e = t * FOURS + g, (b + g) % 2
                        act.wait_ge(s("wt_turned"), n + 1)
                        if not (isinstance(t, int) and t * FOURS + g < 2):
                            act.wait_ge(s("four_done"), n - 1)
                        m = min(4, TILES - 4 * g)
                        a.copy(wt[:, e, 0:m].rearrange("p i d -> p (i d)"), ps[:, 4 + e, 0:m * P]).then_inc(s("wt_copied"), 1)

                def build(j, b, n):
                    for u in range(TILE_HOTS * 2):
                        if u == 0 and later(j, 2):
                            act.wait_ge(s(f"a_stored{b}"), n * 16)
                            act.wait_ge(s("wt_turned"), (j - 1) * FOURS)
                        act.wait_ge(s("unit_done"), j * 16 + (u + 1))
                        for k, stage in ((0, stage_a), (1, stage_w)):
                            of = ps[:, (u % 2) * 2:(u % 2) * 2 + 2, k * 2 * WCOLS:(k + 1) * 2 * WCOLS].rearrange("p b (d i) -> p i b d", i=TILES)
                            to = stage[:, b, :, u * 8:(u + 1) * 8].rearrange("p i (b d) -> p i b d", b=2)
                            last = a.copy(to, of)
                        last.then_inc(s("evacuated"), 1)
                        if u % 2 and (not isinstance(j, int) or j):
                            copy_weights(j - 1, 1 - b, u // 2)

                if not general:
                    pairs_loop(act, build)
                    for h in range(TILE_HOTS):
                        copy_weights(TILES - 1, 0, h)

                for ph in (1, 2, 3, 4):
                    if ph < 4:
                        std(ph)
                        if general:
                            with act.Fori(0, TILES) as i:
                                to = rows_all[:, bass.ds(i, 1), 0:P].rearrange("p a f -> p (a f)")
                                relu_row(to, i).then_inc(s("g_h"), 1)
                    if ph < 4 and not general:
                        stages_stored(act, ph)
                        for c in range(SET + 1):
                            if c < SET:
                                if c >= 2:
                                    act.wait_ge(s(f"split_d{ph}"), c - 1)
                                for i in range(SET):
                                    last = relu_row(hbig[:, c % 2, i], c * SET + i)
                                last.then_inc(s(f"split_h{ph}"), 1)
                            if c:
                                act.wait_ge(s(f"split_d{ph}"), c)
                                a.activation(Ha[:, (c - 1) * SET:c * SET, P:2 * P], dbig[:, (c - 1) % 2], ACT.Copy, scale=LOW).then_inc(s(f"h_ready{ph}"), 1)

                    def step(j, k, c, ph=ph):
                        q = c % SLOTS
                        if on(j):
                            if ph == 2:
                                if later(j, SLOTS):
                                    act.wait_ge(s("t_done2"), j - (SLOTS - 1))
                                relu_row(hrow[:, q], j).then_inc(s("hrow_ready"), 1)
                        if on(j) and not general:
                            if ph == 1:
                                copy_turned(act, a.copy, j, k, c, 1)
                            act.wait_ge(s(f"sum_done{ph}"), j + 1)
                            a.copy(row(extra, j), ps[:, c % 2, 2 * P:PARTS])
                            if later(j, SLOTS):
                                act.wait_ge(s(f"agg_ready{ph}"), j - (SLOTS - 1))
                            a.activation(low[:, q], ps[:, c % 2, P:2 * P], ACT.Copy, scale=1.0 / LOW).then_inc(s(f"low_ready{ph}"), 1)
                        if ph != 3 and on(j, 1):
                            t, d = j - 1, c - 1
                            act.wait_ge(s(f"t_done{ph}"), t + 1)
                            if later(t, SLOTS):
                                act.wait_ge(s(f"mm_done{ph}"), t - (SLOTS - 1))
                            n = 2 if ph == 2 else 1
                            a.copy(aggt[:, d % SLOTS, 0:n].rearrange("p a f -> p (a f)"), ps[:, 4 + d % 2, 0:n * P]).then_inc(s(f"aggt_ready{ph}"), 1)
                        if ph == 3 and on(j, 1):
                            t, d = j - 1, c - 1
                            act.wait_ge(s("e_rest"), t + 1)
                            lo = Hb[:, t, P:2 * P] if isinstance(t, int) else Hb[:, bass.ds(t, 1), P:2 * P].rearrange("p a f -> p (a f)")
                            a.activation(lo, upd[:, d % SLOTS, 1], ACT.Copy, scale=LOW).then_inc(s("h_ready4"), 1)
                        if ph == 4 and on(j, 2):
                            t, d = j - 2, c - 2
                            act.wait_ge(s("mm_done4"), t + 1)
                            a.activation(row(OT, t), ps[:, 6 + d % 2, 0:P], ACT.Identity, bias=cols[:, 1:2]).then_inc(s("upd_done4"), 1)

                    if not (general and ph == 3):
                        tiles_loop(act, step, 2)

            branch(act, layers)

            act.wait_ge(s("bvar"), 1)
            a.activation(fin[:, 3:4], fin[:, 2:3], ACT.Sqrt).then_inc(s("bstd"), 1)
            act.wait_ge(s("batch"), 1)

            def last_step(j, k, c):
                if on(j):
                    if later(j, SLOTS):
                        act.wait_ge(s("y_turned"), j - (SLOTS - 1))
                    a.activation(hrow[:, c % SLOTS], row(OT, j), ACT.Relu, bias=fin[:, 7:8], scale=fin[:, 5:6]).then_inc(s("y_ready"), 1)

            tiles_loop(act, last_step, 0)


_INS = ["x", "src", "dst", "edge_weight", "L0_gnn_W", "L0_gnn_W_gate", "L0_gnn_b_gate", "L1_gnn_W", "L1_gnn_b",
        "L2_gnn_W_msg", "L2_gnn_b_msg", "L2_gnn_W_upd", "L2_gnn_b_upd", "L3_gnn_hyperedge_weight", "L3_gnn_W",
        "L3_gnn_b", "L3_gnn_gamma", "L3_gnn_beta"]


def kernel(**inputs):
    import concourse.bacc as bacc
    from concourse.bass_utils import run_bass_kernel_spmd

    nc = bacc.Bacc("TRN2", target_bir_lowering=False, num_devices=1)
    arrays, args = {}, []
    for name in _INS:
        a = np.ascontiguousarray(inputs[name])
        arrays[f"in_{name}"] = a
        args.append(nc.dram_tensor(f"in_{name}", a.shape, mybir.dt.from_np(a.dtype), kind="ExternalInput").ap())
    out = nc.dram_tensor("out_x", (NODES, P), F32, kind="ExternalOutput").ap()
    gnn_kernel(nc, *args, out)
    r = run_bass_kernel_spmd(nc, [arrays], core_ids=[0])
    return r.results[0]["out_x"]
```
